# Optimizing a Trainium2 kernel written in Bass

```python
import numpy as np
import jax
import jax.numpy as jnp

def _softmax(x, axis=-1):
    return jax.nn.softmax(x, axis=axis)

def _gelu(x):
    return jax.nn.gelu(x, approximate=True)

def _silu(x):
    return jax.nn.silu(x)

def _sigmoid(x):
    return jax.nn.sigmoid(x)

def _layernorm(x, axis=-1, eps=1e-05):
    m = jnp.mean(x, axis=axis, keepdims=True)
    v = jnp.var(x, axis=axis, keepdims=True)
    return (x - m) / jnp.sqrt(v + eps)

def _scatter_add(tgt, idx, src, axis=0):
    return tgt.at[idx].add(src)

def _segment_sum(src, seg, n):
    return jax.ops.segment_sum(src, seg, n)
kernel_name = 'mk_adaln_ffn_d1_seqx_r4_c239d6'

def setup_inputs(seed: int=0):
    np.random.seed(seed)
    _w = jnp.asarray

    def _rec_inputs():
        import jax
        import jax.numpy as jnp
        _rk = jax.random.key(seed)
        x = 7.22e-05 + 1 * jax.random.normal(jax.random.fold_in(_rk, 1), (2, 1024, 256), jnp.float32)
        _lenS = 1024 - jax.random.randint(jax.random.fold_in(_rk, 7), (2,), 0, max(1, 1024 // 4) + 1, jnp.int32)
        _lenS2 = 1024 - jax.random.randint(jax.random.fold_in(_rk, 8), (2,), 0, max(1, 1024 // 4) + 1, jnp.int32)
        cond_8 = -0.104238 + 1.01173 * jax.random.normal(jax.random.fold_in(_rk, 11), (2, 8), jnp.float32)
        return (x, cond_8)
    x, cond_8 = _rec_inputs()

    def _L0_cond_setup():
        import jax, jax.numpy as jnp
        import numpy as np
        TOP_K = 2
        NUM_MOE_LAYERS = 12

        def _gemma_mlp(x, gate_w, up_w, down_w):
            g = jnp.einsum('bsh,hi->bsi', x, gate_w)
            u = jnp.einsum('bsh,hi->bsi', x, up_w)
            return jnp.einsum('bsi,ih->bsh', jax.nn.gelu(g, approximate=True) * u, down_w)
        key = jax.random.key(seed)
        ks = jax.random.split(key, 8)
        B, S, H, I, E = (32, 64, 256, 1024, 8)
        std = 0.02
        return {'x': jax.random.normal(ks[0], (B, S, H), jnp.float32), 'router_logits': jax.random.normal(ks[1], (B, E), jnp.float32), 'skill_gate': jax.random.normal(ks[2], (E, H, I), jnp.float32) * std, 'skill_up': jax.random.normal(ks[3], (E, H, I), jnp.float32) * std, 'skill_down': jax.random.normal(ks[4], (E, I, H), jnp.float32) * std, 'shared_gate': jax.random.normal(ks[5], (H, I), jnp.float32) * std, 'shared_up': jax.random.normal(ks[6], (H, I), jnp.float32) * std, 'shared_down': jax.random.normal(ks[7], (I, H), jnp.float32) * std}
    _L0_cond_all = _L0_cond_setup()
    _L0_cond_in = {k: v for k, v in _L0_cond_all.items() if k in ('skill_gate', 'skill_up', 'skill_down', 'shared_gate', 'shared_up', 'shared_down')}
    del _L0_cond_all

    def _L0_ffn_setup():
        import jax, jax.numpy as jnp
        import numpy as np
        B, S, H = (8, 1024, 256)
        NAV = 128
        E = 8
        F = 2 * H
        key = jax.random.key(seed)
        ks = jax.random.split(key, 12)

        def w(k, shape, fan_in):
            return jax.random.normal(k, shape, dtype=jnp.float32) / np.sqrt(fan_in)
        return {'hidden_states': jax.random.normal(ks[0], (B, S, H), dtype=jnp.float32), 'Wp1': w(ks[1], (H, NAV), H), 'bp1': jnp.zeros((NAV,), jnp.float32), 'Wp2': w(ks[2], (NAV, E), NAV), 'bp2': jnp.zeros((E,), jnp.float32), 'W1': w(ks[3], (E, H, F), H), 'b1': jnp.zeros((E, F), jnp.float32), 'W2': w(ks[4], (E, F, H), F), 'b2': jnp.zeros((E, H), jnp.float32), 'Wo': w(ks[5], (H, H), H), 'bo': jnp.zeros((H,), jnp.float32)}
    _L0_ffn_all = _L0_ffn_setup()
    _L0_ffn_in = {k: v for k, v in _L0_ffn_all.items() if k in ('Wp1', 'bp1', 'Wp2', 'bp2', 'W1', 'b1', 'W2', 'b2', 'Wo', 'bo')}
    del _L0_ffn_all
    return {'x': x, 'cond_8': cond_8, 'L0_cond_skill_gate': _L0_cond_in['skill_gate'], 'L0_cond_skill_up': _L0_cond_in['skill_up'], 'L0_cond_skill_down': _L0_cond_in['skill_down'], 'L0_cond_shared_gate': _L0_cond_in['shared_gate'], 'L0_cond_shared_up': _L0_cond_in['shared_up'], 'L0_cond_shared_down': _L0_cond_in['shared_down'], 'L0_ffn_Wp1': _L0_ffn_in['Wp1'], 'L0_ffn_bp1': _L0_ffn_in['bp1'], 'L0_ffn_Wp2': _L0_ffn_in['Wp2'], 'L0_ffn_bp2': _L0_ffn_in['bp2'], 'L0_ffn_W1': _L0_ffn_in['W1'], 'L0_ffn_b1': _L0_ffn_in['b1'], 'L0_ffn_W2': _L0_ffn_in['W2'], 'L0_ffn_b2': _L0_ffn_in['b2'], 'L0_ffn_Wo': _L0_ffn_in['Wo'], 'L0_ffn_bo': _L0_ffn_in['bo']}

def reference(x, cond_8, L0_cond_skill_gate, L0_cond_skill_up, L0_cond_skill_down, L0_cond_shared_gate, L0_cond_shared_up, L0_cond_shared_down, L0_ffn_Wp1, L0_ffn_bp1, L0_ffn_Wp2, L0_ffn_bp2, L0_ffn_W1, L0_ffn_b1, L0_ffn_W2, L0_ffn_b2, L0_ffn_Wo, L0_ffn_bo):
    import jax
    import jax.numpy as jnp

    def _L0_cond_ref(x, router_logits, skill_gate, skill_up, skill_down, shared_gate, shared_up, shared_down):
        import jax, jax.numpy as jnp
        import numpy as np
        TOP_K = 2
        NUM_MOE_LAYERS = 12

        def _gemma_mlp(x, gate_w, up_w, down_w):
            g = jnp.einsum('bsh,hi->bsi', x, gate_w)
            u = jnp.einsum('bsh,hi->bsi', x, up_w)
            return jnp.einsum('bsi,ih->bsh', jax.nn.gelu(g, approximate=True) * u, down_w)
        B = x.shape[0]
        E = skill_gate.shape[0]
        rw = jax.nn.softmax(router_logits.astype(jnp.float32), axis=-1)
        w, sel = jax.lax.top_k(rw, TOP_K)
        w = w / w.sum(axis=-1, keepdims=True)
        w = w.astype(x.dtype)
        scale = 1.0 / NUM_MOE_LAYERS
        w = scale * w + (1.0 - scale) * jax.lax.stop_gradient(w)
        dense_w = jnp.zeros((B, E), x.dtype).at[jnp.arange(B)[:, None], sel].add(w)

        def step(acc, params):
            g, u, d, we = params
            return (acc + we[:, None, None] * _gemma_mlp(x, g, u, d), None)
        out, _ = jax.lax.scan(step, jnp.zeros_like(x), (skill_gate, skill_up, skill_down, dense_w.T))
        out = out + _gemma_mlp(x, shared_gate, shared_up, shared_down)
        return out

    def _L0_ffn_ref(hidden_states, Wp1, bp1, Wp2, bp2, W1, b1, W2, b2, Wo, bo):
        import jax, jax.numpy as jnp
        import numpy as np
        B, S, H = (8, 1024, 256)
        NAV = 128
        E = 8
        F = 2 * H
        last = hidden_states[:, -1, :]
        logits = jax.nn.gelu(last @ Wp1 + bp1, approximate=False) @ Wp2 + bp2
        action_probs = jax.nn.softmax(logits, axis=-1)
        sel = jnp.argmax(action_probs, axis=-1)
        w1 = W1[sel]
        w2 = W2[sel]
        h = jax.nn.gelu(jnp.einsum('bsh,bhf->bsf', hidden_states, w1) + b1[sel][:, None, :], approximate=False)
        reasoned = jnp.einsum('bsf,bfh->bsh', h, w2) + b2[sel][:, None, :]
        out = reasoned @ Wo + bo
        return hidden_states + 0.3 * out
    x = x + _L0_ffn_ref(_L0_cond_ref(x, cond_8, L0_cond_skill_gate, L0_cond_skill_up, L0_cond_skill_down, L0_cond_shared_gate, L0_cond_shared_up, L0_cond_shared_down), L0_ffn_Wp1, L0_ffn_bp1, L0_ffn_Wp2, L0_ffn_bp2, L0_ffn_W1, L0_ffn_b1, L0_ffn_W2, L0_ffn_b2, L0_ffn_Wo, L0_ffn_bo)
    return x

_drawn_inputs = setup_inputs


def setup_inputs(seed=0):
    import zlib

    import numpy as np

    out = dict(_drawn_inputs(seed))
    spreads = {'L0_ffn_bp1': (0.0, 0.1),
     'L0_ffn_bp2': (0.0, 0.1),
     'L0_ffn_b1': (0.0, 0.515),
     'L0_ffn_b2': (0.0, 0.273),
     'L0_ffn_bo': (0.0, 0.275)}
    factors = {'L0_ffn_W1': 8.0, 'L0_ffn_W2': 3.298}
    for name, (base, spread) in spreads.items():
        noise = np.random.default_rng([zlib.crc32(name.encode()), seed]).standard_normal(out[name].shape)
        drawn = base * np.exp(spread * noise) if base else spread * noise
        out[name] = jnp.asarray(drawn.astype(out[name].dtype))
    for name, factor in factors.items():
        out[name] = (out[name] * factor).astype(out[name].dtype)
    return out
```

```python
import concourse.bass as bass
from concourse import mybir
from contextlib import ExitStack


def adaln_moe_ffn(
    nc: bass.Bass,
    x: bass.AP,
    cond_8: bass.AP,
    skill_gate: bass.AP,
    skill_up: bass.AP,
    skill_down: bass.AP,
    shared_gate: bass.AP,
    shared_up: bass.AP,
    shared_down: bass.AP,
    Wp1: bass.AP,
    bp1: bass.AP,
    Wp2: bass.AP,
    bp2: bass.AP,
    W1: bass.AP,
    b1: bass.AP,
    W2: bass.AP,
    b2: bass.AP,
    Wo: bass.AP,
    bo: bass.AP,
    out: bass.AP,
):
    fp32 = mybir.dt.float32
    fp32r = mybir.dt.float32r
    u32 = mybir.dt.uint32
    ALU = mybir.AluOpType
    ACT = mybir.ActivationFunctionType
    AX = mybir.AxisListType

    P = 128
    B, S, H = x.shape
    E, _, I = skill_gate.shape
    F = W1.shape[2]
    KH = H // P
    HALF = S // 2
    IT = I // P
    FT = F // P
    TT = S // P
    TH = HALF // P
    CHUNKS = IT // 2
    CW = 2 * P
    PARTS = 2 * KH + 2
    STEPS = 3
    TILES = 2 * IT
    LAG = 2
    AHEAD = 2
    RING = 4
    TOP_K = 2
    SCALE = 1.0 / 12
    MIX = 0.3
    LOADS = 3 * 16
    assert H == CW and HALF == 512 and TILES % RING == 0 and B * E <= P

    ctx = ExitStack()
    with ctx:
        ctx.enter_context(nc.allow_non_contiguous_dma(reason="biases onto partitions, a few KB"))

        def sb(name, shape, dt=fp32):
            return ctx.enter_context(nc.sbuf_tensor(name, shape, dt))

        def sem(name):
            return ctx.enter_context(nc.semaphore(name))

        w_raw = sb("w_raw", [P, CHUNKS, PARTS, CW])
        w_hi = sb("w_hi", [P, CHUNKS, PARTS, CW], fp32r)
        w_lo = sb("w_lo", [P, CHUNKS, PARTS, CW], fp32r)
        x_raw = sb("x_raw", [P, TT, H])
        xb = sb("xb", [P, TT, H])
        xT_hi = sb("xT_hi", [P, 2, KH, HALF], fp32r)
        xT_lo = sb("xT_lo", [P, 2, KH, HALF], fp32r)
        act = sb("act", [P, 2, HALF])
        h32 = sb("h32", [P, 2, HALF])
        h_hi = sb("h_hi", [P, RING, HALF], fp32r)
        h_lo = sb("h_lo", [P, RING, HALF], fp32r)
        c32 = sb("c32", [P, 2, KH, HALF])
        c_hi = sb("c_hi", [P, 2, KH, HALF], fp32r)
        c_lo = sb("c_lo", [P, 2, KH, HALF], fp32r)
        f_raw = sb("f_raw", [P, KH * F + FT * H])
        f_hi = sb("f_hi", [P, KH * F + FT * H], fp32r)
        f_lo = sb("f_lo", [P, KH * F + FT * H], fp32r)
        r_hi = sb("r_hi", [P, 2, KH, HALF], fp32r)
        r_lo = sb("r_lo", [P, 2, KH, HALF], fp32r)
        wo_raw = sb("wo_raw", [P, KH, H])
        wo_hi = sb("wo_hi", [P, KH, H], fp32r)
        wo_lo = sb("wo_lo", [P, KH, H], fp32r)
        ident = sb("ident", [P, P])
        zeros = sb("zeros", [P, HALF], mybir.dt.bfloat16)
        ident_r = sb("ident_r", [P, P], fp32r)
        wp1 = sb("wp1", [P, KH, P])
        wp2 = sb("wp2", [P, E])
        bp1_c = sb("bp1_c", [P, 1])
        bp2_r = sb("bp2_r", [1, E])
        b1_c = sb("b1_c", [P, FT])
        b2_c = sb("b2_c", [P, KH])
        b2_m = sb("b2_m", [P, KH])
        bo_b = sb("bo_b", [P, H])
        bo_m = sb("bo_m", [P, H])
        logit = sb("logit", [P, B, E])
        top = sb("top", [P, B, 8])
        neg = sb("neg", [P, B])
        prob = sb("prob", [P, B, E])
        denom = sb("denom", [P, B])
        top_i = sb("top_i", [P, B, 8], u32)
        wsum = sb("wsum", [P, B])
        wnorm = sb("wnorm", [P, B, TOP_K])
        wmix = sb("wmix", [P, B, TOP_K])
        gain = sb("gain", [P, B * STEPS])
        nav = sb("nav", [P, 1])
        rl = sb("rl", [1, E])
        rtop = sb("rtop", [1, 8])
        rneg = sb("rneg", [1, 1])
        rexp = sb("rexp", [1, E])
        rsum = sb("rsum", [1, 1])
        rprob = sb("rprob", [1, E])
        rptop = sb("rptop", [1, 8])
        rsel = sb("rsel", [1, 8], u32)

        f1_hi = xT_hi[:, :, :, :].rearrange("p t k n -> p (t k) n")
        f1_lo = xT_lo[:, :, :, :].rearrange("p t k n -> p (t k) n")
        hf_hi = (h_hi, f1_hi)
        hf_lo = (h_lo, f1_lo)

        acc = ctx.enter_context(nc.psum_tensor("acc", [P, 2, KH, HALF], fp32))
        turn = ctx.enter_context(nc.psum_tensor("turn", [P, 4, HALF], fp32))

        cond_loaded = sem("cond_loaded")
        consts_loaded = sem("consts_loaded")
        pool_consts_loaded = sem("pool_consts_loaded")
        router_loaded = sem("router_loaded")
        ident_step = sem("ident_step")
        ident_ready = sem("ident_ready")
        wo_step = sem("wo_step")
        wo_split = sem("wo_split")
        route_dve = sem("route_dve")
        route_neg = sem("route_neg")
        route_exp = sem("route_exp")
        routed = sem("routed")
        x_loaded = [sem(f"x_loaded{t}") for t in range(2)]
        xb_ready = sem("xb_ready")
        x_transposed = sem("x_transposed")
        x_hi_done = sem("x_hi_done")
        x_split = sem("x_split")
        w_loaded = [sem(f"w_loaded{c}") for c in range(CHUNKS)]
        w_hi_done = sem("w_hi_done")
        w_split = sem("w_split")
        gate_done = sem("gate_done")
        up_done = sem("up_done")
        gelu_done = sem("gelu_done")
        h_done = sem("h_done")
        h_hi_done = sem("h_hi_done")
        h_split = sem("h_split")
        down_done = sem("down_done")
        c_copied = sem("c_copied")
        c_hi_done = sem("c_hi_done")
        c_split = sem("c_split")
        nav_done = sem("nav_done")
        nav_gelu = sem("nav_gelu")
        rlogit_done = sem("rlogit_done")
        rneg_done = sem("rneg_done")
        rexp_done = sem("rexp_done")
        router_dve = sem("router_dve")
        waited_apart = sem("waited_apart")
        f_loaded = sem("f_loaded")
        fb_loaded = sem("fb_loaded")
        f_hi_done = sem("f_hi_done")
        f_split = sem("f_split")
        b2_done = sem("b2_done")
        inner_done = sem("inner_done")
        inner_gelu = sem("inner_gelu")
        inner_hi = sem("inner_hi")
        inner_split = sem("inner_split")
        r_done = sem("r_done")
        r_evac = sem("r_evac")
        r_hi_done = sem("r_hi_done")
        r_split = sem("r_split")
        sum_done = sem("sum_done")
        out_ready = sem("out_ready")
        out_stored = [sem(f"out_stored{q}") for q in range(4)]

        block = ctx.enter_context(nc.Block())

        def wait_apart(eng, semaphore, value):
            eng.wait_ge(semaphore, value)
            eng.sem_inc(waited_apart, 1)

        half_of = lambda n: 1 - n // IT
        x_v = x.rearrange("b (t p) h -> b p t h", p=P)
        out_v = out.rearrange("b (t p) h -> b p t h", p=P)

        @block.sync
        def _(sp):
            def load_chunk(c, gate_w, up_w, down_w):
                sp.dma_start(w_raw[:, c, 0:KH, :],
                             gate_w[:, c * CW:(c + 1) * CW].rearrange("(k p) n -> p k n", p=P)
                             ).then_inc(w_loaded[c], 16)
                sp.dma_start(w_raw[:, c, KH:2 * KH, :],
                             up_w[:, c * CW:(c + 1) * CW].rearrange("(k p) n -> p k n", p=P)
                             ).then_inc(w_loaded[c], 16)
                sp.dma_start(w_raw[:, c, 2 * KH:PARTS, :],
                             down_w[c * CW:(c + 1) * CW, :].rearrange("(t p) n -> p t n", p=P)
                             ).then_inc(w_loaded[c], 16)

            with sp.Fori(0, B) as b:
                sp.wait_ge(x_transposed, 4 * b + 4)
                sp.wait_ge(xb_ready, 4 * b + 4)
                for t in (1, 0):
                    sp.dma_start(x_raw[:, t * TH:(t + 1) * TH, :],
                                 x_v[b, :, t * TH:(t + 1) * TH, :]).then_inc(x_loaded[t], 16)
                for c in range(CHUNKS):
                    sp.wait_ge(w_split, CHUNKS * STEPS * b + c + 1)
                    load_chunk(c, shared_gate, shared_up, shared_down)
                sp.wait_ge(routed, B)
                with sp.Fori(0, TOP_K) as e:
                    k = sp.value_load(top_i[0:1, b, bass.ds(e, 1)], min_val=0, max_val=E - 1)
                    for c in range(CHUNKS):
                        sp.wait_ge(w_split, CHUNKS * (STEPS * b + 1 + e) + c + 1)
                        load_chunk(c, skill_gate[k, :, :], skill_up[k, :, :], skill_down[k, :, :])
                sp.wait_ge(out_ready, 4 * b + 4)
                wait_apart(sp, router_dve, 6 * b + 6)
                k = sp.value_load(rsel[0:1, 0:1], min_val=0, max_val=E - 1)
                sp.dma_start(f_raw[:, 0:KH * F].rearrange("p (k n) -> p k n", k=KH),
                             W1[k, :, :].rearrange("(k p) n -> p k n", p=P)).then_inc(f_loaded, 16)
                sp.dma_start(f_raw[:, KH * F:].rearrange("p (k n) -> p k n", k=FT),
                             W2[k, :, :].rearrange("(k p) n -> p k n", p=P)).then_inc(f_loaded, 16)
                sp.dma_start(b1_c[:, :], b1[k, :].rearrange("(f p) -> p f", p=P)).then_inc(fb_loaded, 16)
                sp.dma_start(b2_c[:, :], b2[k, :].rearrange("(f p) -> p f", p=P)).then_inc(fb_loaded, 16)

        @block.gpsimd
        def _(pool):
            pool.sem_inc(xb_ready, 4)
            pool.memset(zeros[:, :], 0.0).then_inc(ident_ready, 1)
            pool.memset(ident[:, :], 0.0).then_inc(ident_step, 1)
            pool.wait_ge(ident_step, 1)
            pool.affine_select(out=ident[:, :], in_=ident[:, :], compare_op=ALU.not_equal, fill=1.0,
                               base=0, pattern=[[-1, P]], channel_multiplier=1).then_inc(ident_step, 1)
            pool.wait_ge(ident_step, 2)
            pool.tensor_copy(ident_r[:, :], ident[:, :]).then_inc(ident_ready, 1)
            pool.wait_ge(pool_consts_loaded, 32)
            pool.tensor_scalar(bo_m[:, :], bo_b[:, :], MIX, None, ALU.mult).then_inc(wo_step, 1)
            pool.tensor_copy(wo_hi[:, :, :], wo_raw[:, :, :]).then_inc(wo_step, 1)
            pool.wait_ge(wo_step, 2)
            pool.tensor_tensor(wo_lo[:, :, :], wo_raw[:, :, :], wo_hi[:, :, :].bitcast(fp32),
                               ALU.subtract).then_inc(wo_split, 1)
            with pool.Fori(0, B) as b:
                for t in (1, 0):
                    pool.wait_ge(x_loaded[t], 16 * b + 16)
                    for q in (2 * t, 2 * t + 1):
                        pool.wait_ge(out_stored[q], 16 * b + 16)
                    for i in range(t * TH, (t + 1) * TH):
                        last = pool.tensor_tensor(xb[:, i, :], x_raw[:, i, :], bo_m[:, :], ALU.add)
                    last.then_inc(xb_ready, 2)

        @block.scalar
        def _(sc):
            sc.dma_start(logit[:, :, :], cond_8.partition_broadcast(P)).then_inc(cond_loaded, 16)
            sc.dma_start(wo_raw[:, :, :], Wo.rearrange("(k p) n -> p k n", p=P)).then_inc(pool_consts_loaded, 16)
            sc.dma_start(bo_b[:, :], bo.partition_broadcast(P)).then_inc(pool_consts_loaded, 16)
            sc.dma_start(wp1[:, :, :], Wp1.rearrange("(k p) n -> p k n", p=P)).then_inc(router_loaded, 16)
            sc.dma_start(wp2[:, :], Wp2).then_inc(router_loaded, 16)
            sc.dma_start(bp1_c[:, :], bp1.rearrange("(p o) -> p o", o=1)).then_inc(router_loaded, 16)
            sc.dma_start(bp2_r[:, :], bp2.rearrange("(o n) -> o n", o=1)).then_inc(router_loaded, 16)
            sc.wait_ge(route_neg, 1)
            for b in range(B):
                last = sc.activation(prob[:, b, :], logit[:, b, :], ACT.Exp, bias=neg[:, b:b + 1])
            last.then_inc(route_exp, 1)

            def split_chunk(b, j, c):
                sc.wait_ge(w_loaded[c], LOADS * (STEPS * b + j + 1))
                sc.wait_ge(down_done, TILES * (STEPS * b + j) + IT + 2 * c + 2)
                sc.activation(w_hi[:, c, :, :], w_raw[:, c, :, :], ACT.Copy).then_inc(w_hi_done, 1)

            def tile(b, j, n):
                done = TILES * (STEPS * b + j) + n
                sc.wait_ge(gate_done, done + 1)
                sc.wait_ge(h_done, done + 1)
                sc.activation(act[:, n % 2, :], turn[:, 2 * (n % 2), :], ACT.Gelu_apprx_tanh
                              ).then_inc(gelu_done, 1)

            def step(b, j, last=False):
                for n in range(TILES):
                    tile(b, j, n)
                    if n == 1:
                        split_chunk(b, j, CHUNKS - 1)
                    if not last and n in (11, 13, 15):
                        split_chunk(b, j + 1, (n - 11) // 2)
                    if last and n == IT + 3:
                        sc.wait_ge(nav_done, b + 1)
                        sc.activation(nav[:, :], acc[:, 1, 0, 0:1], ACT.Gelu, bias=bp1_c[:, :]
                                      ).then_inc(nav_gelu, 1)
                    if last and n == IT + 5:
                        sc.wait_ge(rneg_done, b + 1)
                        sc.activation(rexp[:, :], rl[:, :], ACT.Exp, bias=rneg[:, :],
                                      accum_out=rsum[:, :]).then_inc(rexp_done, 1)
                    if last and n == TILES - 1:
                        sc.wait_ge(f_loaded, 32 * b + 32)
                        sc.activation(f_hi[:, :], f_raw[:, :], ACT.Copy).then_inc(f_hi_done, 1)

            sc.sem_inc(gelu_done, AHEAD)
            for q in range(4):
                sc.sem_inc(out_stored[q], 16)
            sc.wait_ge(router_loaded, 64)
            with sc.Fori(0, B) as b:
                for u, t in enumerate((1, 0)):
                    if t == 0:
                        split_chunk(b, 0, 0)
                    for k in range(KH):
                        sc.wait_ge(x_transposed, 4 * b + 4 + 2 * u + k + 1)
                        sc.activation(xT_hi[:, t, k, :], turn[:, 2 * u + k, :], ACT.Copy).then_inc(x_hi_done, 1)
                split_chunk(b, 0, 1)
                split_chunk(b, 0, 2)
                with sc.Fori(0, STEPS - 1) as j:
                    step(b, j)
                step(b, STEPS - 1, last=True)
                sc.wait_ge(fb_loaded, 32 * b + 32)
                for u in range(2):
                    for f in range(FT):
                        i = u * FT + f
                        sc.wait_ge(inner_done, 2 * FT * b + i + 1)
                        if i < 2:
                            sc.wait_ge(h_done, TILES * STEPS * (b + 1) + AHEAD - 1 + i)
                        else:
                            sc.wait_ge(inner_split, 2 * FT * b + i - 1)
                        sc.activation(act[:, i % 2, :], turn[:, f, :], ACT.Gelu, bias=b1_c[:, f:f + 1]
                                      ).then_inc(inner_gelu, 1)
                sc.wait_ge(b2_done, b + 1)
                for u in range(2):
                    for m in range(KH):
                        i = u * KH + m
                        sc.wait_ge(r_done, 4 * b + i + 1)
                        if i < 2:
                            sc.wait_ge(inner_split, 2 * FT * b + 2 * FT - 1 + i)
                        else:
                            sc.wait_ge(r_split, 4 * b + i - 1)
                        sc.activation(act[:, i % 2, :], acc[:, 1 - u, m, :], ACT.Identity,
                                      bias=b2_m[:, m:m + 1], scale=MIX).then_inc(r_evac, 1)
                for i, q in enumerate((2, 3, 0, 1)):
                    sc.wait_ge(out_ready, 4 * b + 4 + i + 1)
                    sc.dma_start(out_v[b, :, 2 * q:2 * q + 2, :], xb[:, 2 * q:2 * q + 2, :]
                                 ).then_inc(out_stored[q], 16)
            for q in range(4):
                sc.wait_ge(out_stored[q], 16 * B + 16)

        @block.vector
        def _(ve):
            ve.sem_inc(w_split, CHUNKS)
            ve.sem_inc(h_done, AHEAD)
            ve.sem_inc(out_ready, 4)
            steps = [0]

            def then(ins):
                steps[0] += 1
                ins.then_inc(route_dve, 1)
                ve.wait_ge(route_dve, steps[0])

            ve.memset(gain[:, :], 1.0).then_inc(route_dve, 1)
            steps[0] += 1
            ve.wait_ge(cond_loaded, 16)
            for b in range(B):
                then(ve.max(top[:, b, :], logit[:, b, :]))
                last = ve.tensor_scalar(neg[:, b:b + 1], top[:, b, 0:1], -1.0, None, ALU.mult)
            last.then_inc(route_neg, 1)
            ve.wait_ge(route_exp, 1)
            then(ve.reduce_sum(denom[:, :], prob[:, :, :], AX.X))
            then(ve.reciprocal(denom[:, :], denom[:, :]))
            for b in range(B):
                then(ve.tensor_scalar(prob[:, b, :], prob[:, b, :], denom[:, b:b + 1], None, ALU.mult))
                then(ve.max(top[:, b, :], prob[:, b, :]))
                then(ve.max_index(top_i[:, b, :], top[:, b, :], prob[:, b, :]))
            then(ve.reduce_sum(wsum[:, :], top[:, :, 0:TOP_K], AX.X))
            then(ve.reciprocal(wsum[:, :], wsum[:, :]))
            for b in range(B):
                then(ve.tensor_scalar(wnorm[:, b, :], top[:, b, 0:TOP_K], wsum[:, b:b + 1], None, ALU.mult))
                then(ve.tensor_scalar(wmix[:, b, :], wnorm[:, b, :], 1.0 - SCALE, None, ALU.mult))
                ve.scalar_tensor_tensor(gain[:, b * STEPS + 1:b * STEPS + 1 + TOP_K], wnorm[:, b, :],
                                        SCALE, wmix[:, b, :], ALU.mult, ALU.add).then_inc(routed, 1)
            ve.wait_ge(routed, B)

            def split_chunk(b, j, c):
                ve.wait_ge(w_hi_done, CHUNKS * (STEPS * b + j) + c + 1)
                ve.tensor_tensor(w_lo[:, c, :, :], w_raw[:, c, :, :],
                                 w_hi[:, c, :, :].bitcast(fp32), ALU.subtract).then_inc(w_split, 1)

            def tile(b, j, n):
                done = TILES * (STEPS * b + j) + n
                ve.wait_ge(gelu_done, done + AHEAD + 1)
                ve.wait_ge(up_done, done + 1)
                s = n % 2
                ve.scalar_tensor_tensor(h32[:, s, :], act[:, s, :], gain[:, bass.ds(b * STEPS + j, 1)],
                                        turn[:, 2 * s + 1, :], ALU.mult, ALU.mult).then_inc(h_done, 1)
                ve.wait_ge(h_done, done + AHEAD + 1)
                ve.wait_ge(down_done, done + TILES - RING + 1)
                ve.tensor_copy(h_hi[:, n % RING, :], h32[:, s, :]).then_inc(h_hi_done, 1)
                ve.wait_ge(h_hi_done, done + 1)
                ve.tensor_tensor(h_lo[:, n % RING, :], h32[:, s, :], h_hi[:, n % RING, :].bitcast(fp32),
                                 ALU.subtract).then_inc(h_split, 1)

            def take_moe(b, u):
                t = 1 - u
                ve.wait_ge(down_done, TILES + TILES * STEPS * b + TILES * (STEPS - 1) + IT * (u + 1))
                ve.tensor_copy(c32[:, t, :, :], acc[:, t, :, :]).then_inc(c_copied, 1)
                ve.wait_ge(c_copied, 2 * b + u + 1)
                ve.tensor_copy(c_hi[:, t, :, :], c32[:, t, :, :]).then_inc(c_hi_done, 1)
                ve.wait_ge(c_hi_done, 2 * b + u + 1)
                ve.tensor_tensor(c_lo[:, t, :, :], c32[:, t, :, :], c_hi[:, t, :, :].bitcast(fp32),
                                 ALU.subtract).then_inc(c_split, 1)

            def router_logits(b):
                ve.wait_ge(rlogit_done, b + 1)
                ve.tensor_tensor(rl[:, :], acc[0:1, 1, 1, 0:E], bp2_r[:, :], ALU.add).then_inc(router_dve, 1)
                wait_apart(ve, router_dve, 6 * b + 1)
                ve.max(rtop[:, :], rl[:, :]).then_inc(router_dve, 1)
                ve.wait_ge(router_dve, 6 * b + 2)
                ve.tensor_scalar(rneg[:, :], rtop[:, 0:1], -1.0, None, ALU.mult).then_inc(rneg_done, 1)

            def router_choice(b):
                ve.wait_ge(rexp_done, b + 1)
                ve.reciprocal(rsum[:, :], rsum[:, :]).then_inc(router_dve, 1)
                ve.wait_ge(router_dve, 6 * b + 3)
                ve.tensor_scalar(rprob[:, :], rexp[:, :], rsum[:, :], None, ALU.mult).then_inc(router_dve, 1)
                wait_apart(ve, router_dve, 6 * b + 4)
                ve.max(rptop[:, :], rprob[:, :]).then_inc(router_dve, 1)
                wait_apart(ve, router_dve, 6 * b + 5)
                ve.max_index(rsel[:, :], rptop[:, :], rprob[:, :]).then_inc(router_dve, 1)

            def step(b, j, last=False):
                for n in range(TILES):
                    tile(b, j, n)
                    if n == 1:
                        split_chunk(b, j, CHUNKS - 1)
                    if not last and n in (11, 13, 15):
                        split_chunk(b, j + 1, (n - 11) // 2)
                    if last and n == IT + 1:
                        take_moe(b, 0)
                    if last and n == IT + 4:
                        router_logits(b)
                    if last and n == IT + 5:
                        router_choice(b)
                    if last and n == TILES - 1:
                        ve.wait_ge(f_hi_done, b + 1)
                        ve.tensor_tensor(f_lo[:, :], f_raw[:, :], f_hi[:, :].bitcast(fp32),
                                         ALU.subtract).then_inc(f_split, 1)

            with ve.Fori(0, B) as b:
                for u, t in enumerate((1, 0)):
                    if t == 0:
                        split_chunk(b, 0, 0)
                    for k in range(KH):
                        ve.wait_ge(x_hi_done, 4 * b + 2 * u + k + 1)
                        ve.tensor_tensor(xT_lo[:, t, k, :], turn[:, 2 * u + k, :],
                                         xT_hi[:, t, k, :].bitcast(fp32), ALU.subtract).then_inc(x_split, 1)
                split_chunk(b, 0, 1)
                split_chunk(b, 0, 2)
                with ve.Fori(0, STEPS - 1) as j:
                    step(b, j)
                step(b, STEPS - 1, last=True)
                take_moe(b, 1)
                for u in range(2):
                    t = 1 - u
                    for f in range(FT):
                        i = u * FT + f
                        ve.wait_ge(inner_gelu, 2 * FT * b + i + 1)
                        ve.tensor_copy(hf_hi[t][:, f, :], act[:, i % 2, :]).then_inc(inner_hi, 1)
                        ve.wait_ge(inner_hi, 2 * FT * b + i + 1)
                        ve.tensor_tensor(hf_lo[t][:, f, :], act[:, i % 2, :], hf_hi[t][:, f, :].bitcast(fp32),
                                         ALU.subtract).then_inc(inner_split, 1)
                    if u == 0:
                        ve.wait_ge(fb_loaded, 32 * b + 32)
                        ve.tensor_scalar(b2_m[:, :], b2_c[:, :], MIX, None, ALU.mult).then_inc(b2_done, 1)
                for u in range(2):
                    t = 1 - u
                    for m in range(KH):
                        i = u * KH + m
                        ve.wait_ge(r_evac, 4 * b + i + 1)
                        ve.tensor_copy(r_hi[:, t, m, :], act[:, i % 2, :]).then_inc(r_hi_done, 1)
                        ve.wait_ge(r_hi_done, 4 * b + i + 1)
                        ve.tensor_tensor(r_lo[:, t, m, :], act[:, i % 2, :], r_hi[:, t, m, :].bitcast(fp32),
                                         ALU.subtract).then_inc(r_split, 1)
                ve.wait_ge(xb_ready, 4 * b + 8)
                for i, q in enumerate((2, 3, 0, 1)):
                    ve.wait_ge(sum_done, 4 * b + i + 1)
                    ve.tensor_tensor(xb[:, 2 * q:2 * q + 2, :],
                                     turn[:, i, :].rearrange("p (t h) -> p t h", h=H),
                                     xb[:, 2 * q:2 * q + 2, :], ALU.add).then_inc(out_ready, 1)

        @block.tensor
        def _(pe):
            def product(o, terms, start, stop):
                passes = [(l, r) for lh, ll, rh, rl_ in terms for l, r in ((ll, rh), (lh, rl_), (lh, rh))]
                for i, (l, r) in enumerate(passes):
                    ins = pe.matmul(o, l, r, start=start and i == 0, stop=stop and i == len(passes) - 1,
                                    skip_group_check=True)
                return ins

            def gate_up(b, j, n):
                done = TILES * (STEPS * b + j) + n
                c, i, t, s = n % IT // 2, n % 2, half_of(n), n % 2
                if n < IT and n % 2 == 0:
                    pe.wait_ge(w_split, CHUNKS + CHUNKS * (STEPS * b + j) + c + 1)
                for part, ready, free in ((0, gate_done, gelu_done), (1, up_done, h_done)):
                    pe.wait_ge(free, done + 1)
                    product(turn[:, 2 * s + part, :],
                            [(w_hi[:, c, part * KH + k, i * P:(i + 1) * P],
                              w_lo[:, c, part * KH + k, i * P:(i + 1) * P],
                              xT_hi[:, t, k, :], xT_lo[:, t, k, :]) for k in range(KH)],
                            True, True).then_inc(ready, 1)

            def down(b, j, n, stop=False):
                c, i, t = n % IT // 2, n % 2, half_of(n)
                pe.wait_ge(h_split, TILES * (STEPS * b + j) + n + 1)
                for m in range(KH):
                    last = product(acc[:, t, m, :],
                                   [(w_hi[:, c, 2 * KH + i, m * P:(m + 1) * P],
                                     w_lo[:, c, 2 * KH + i, m * P:(m + 1) * P],
                                     h_hi[:, n % RING, :], h_lo[:, n % RING, :])], False, stop)
                last.then_inc(down_done, 1)

            def inner(b, u, f):
                t = 1 - u
                pe.wait_ge(c_split, 2 * b + u + 1)
                if u:
                    pe.wait_ge(inner_gelu, 2 * FT * b + f + 1)
                else:
                    pe.wait_ge((gelu_done, h_done)[f % 2], TILES * STEPS * (b + 1) + AHEAD - 1 + f // 2)
                product(turn[:, f, :],
                        [(f_hi[:, k * F + f * P:k * F + (f + 1) * P],
                          f_lo[:, k * F + f * P:k * F + (f + 1) * P],
                          c_hi[:, t, k, :], c_lo[:, t, k, :]) for k in range(KH)],
                        True, True).then_inc(inner_done, 1)

            def outer(b, u, m):
                t = 1 - u
                pe.wait_ge(inner_split, 2 * FT * b + FT * (u + 1))
                product(acc[:, t, m, :],
                        [(f_hi[:, KH * F + k * H + m * P:KH * F + k * H + (m + 1) * P],
                          f_lo[:, KH * F + k * H + m * P:KH * F + k * H + (m + 1) * P],
                          hf_hi[t][:, k, :], hf_lo[t][:, k, :]) for k in range(FT)],
                        True, True).then_inc(r_done, 1)

            def final(b, u, q):
                t = 1 - u
                bank = 2 * u + q % 2
                pe.wait_ge(r_split, 4 * b + 2 * (u + 1))
                pe.wait_ge(inner_gelu, 2 * FT * b + FT + bank + 1)
                for i in range(2):
                    tok = slice((2 * (q % 2) + i) * P, (2 * (q % 2) + i + 1) * P)
                    product(turn[:, bank, i * H:(i + 1) * H],
                            [(r_hi[:, t, k, tok], r_lo[:, t, k, tok], wo_hi[:, k, :], wo_lo[:, k, :])
                             for k in range(KH)], True, False)
                    for k in range(KH):
                        for part in (c_lo, c_hi):
                            last = pe.matmul(turn[:, bank, i * H + k * P:i * H + (k + 1) * P],
                                             part[:, t, k, tok], ident_r[:, :], start=False,
                                             stop=k == KH - 1 and part is c_hi, skip_group_check=True)
                last.then_inc(sum_done, 1)

            pe.sem_inc(down_done, TILES)
            pe.sem_inc(x_transposed, 4)
            pe.wait_ge(ident_ready, 2)
            with pe.Fori(0, B) as b:
                pe.wait_ge(out_ready, 4 * b + 4)
                for u, t in enumerate((1, 0)):
                    pe.wait_ge(x_loaded[t], 16 * b + 16)
                    for k in range(KH):
                        for i in range(TH):
                            last = pe.transpose(turn[:, 2 * u + k, i * P:(i + 1) * P],
                                                x_raw[:, t * TH + i, k * P:(k + 1) * P], ident[:, :])
                        last.then_inc(x_transposed, 1)
                for t in (1, 0):
                    for m in range(KH):
                        pe.matmul(acc[:, t, m, :], zeros[:, 0:P], zeros[:, :], start=True, stop=False,
                                  skip_group_check=True)
                pe.wait_ge(x_split, 4 * b + KH)
                gate_up(b, 0, 0)
                pe.wait_ge(x_split, 4 * b + 2 * KH)
                gate_up(b, 0, 1)
                with pe.Fori(0, STEPS - 1) as j:
                    for n in range(LAG, TILES):
                        gate_up(b, j, n)
                        down(b, j, n - LAG)
                    for n in range(LAG):
                        gate_up(b, j + 1, n)
                        down(b, j, TILES - LAG + n)
                for n in range(LAG, TILES):
                    gate_up(b, STEPS - 1, n)
                    if n == IT + 3:
                        pe.wait_ge(c_copied, 2 * b + 1)
                        pe.wait_ge(router_loaded, 64)
                        for k in range(KH):
                            last = pe.matmul(acc[:, 1, 0, 0:1], wp1[:, k, :], c32[:, 1, k, HALF - 1:HALF],
                                             start=k == 0, stop=k == KH - 1, skip_group_check=True)
                        last.then_inc(nav_done, 1)
                    if n == IT + 4:
                        pe.wait_ge(nav_gelu, b + 1)
                        pe.matmul(acc[0:1, 1, 1, 0:E], nav[:, :], wp2[:, :], start=True, stop=True,
                                  skip_group_check=True).then_inc(rlogit_done, 1)
                    down(b, STEPS - 1, n - LAG, stop=n - LAG in (IT - 1, TILES - 1))
                down(b, STEPS - 1, TILES - 2)
                pe.wait_ge(f_split, b + 1)
                inner(b, 0, 0)
                inner(b, 0, 1)
                down(b, STEPS - 1, TILES - 1, stop=True)
                inner(b, 0, 2)
                inner(b, 0, 3)
                for f in range(FT):
                    inner(b, 1, f)
                for u in range(2):
                    for m in range(KH):
                        outer(b, u, m)
                pe.wait_ge(wo_split, 1)
                for u in range(2):
                    for q in (2 * (1 - u), 2 * (1 - u) + 1):
                        final(b, u, q)


_INS = ["x", "cond_8", "L0_cond_skill_gate", "L0_cond_skill_up", "L0_cond_skill_down",
        "L0_cond_shared_gate", "L0_cond_shared_up", "L0_cond_shared_down",
        "L0_ffn_Wp1", "L0_ffn_bp1", "L0_ffn_Wp2", "L0_ffn_bp2", "L0_ffn_W1", "L0_ffn_b1",
        "L0_ffn_W2", "L0_ffn_b2", "L0_ffn_Wo", "L0_ffn_bo"]
_OUTS = [((2, 1024, 256), "float32")]


def kernel(**inputs):
    import numpy as _np
    import concourse.bacc as _bacc
    from concourse import mybir as _mybir
    from concourse.bass_utils import run_bass_kernel_spmd as _run

    nc = _bacc.Bacc("TRN2", target_bir_lowering=False, num_devices=1)
    arrays, args = {}, []
    for name in _INS:
        a = _np.ascontiguousarray(inputs[name])
        arrays[f"in_{name}_dram"] = a
        args.append(nc.dram_tensor(f"in_{name}_dram", a.shape, _mybir.dt.from_np(a.dtype), kind="ExternalInput").ap())
    for i, (shape, dtype) in enumerate(_OUTS):
        dt = _mybir.dt.from_np(_np.dtype(dtype))
        args.append(nc.dram_tensor(f"out_{i}_dram", shape, dt, kind="ExternalOutput").ap())
    adaln_moe_ffn(nc, *args)
    r = _run(nc, [arrays], core_ids=[0])
    return r.results[0]["out_0_dram"]
```

```python
import concourse.bass as bass
from concourse import mybir
from contextlib import ExitStack


def adaln_moe_ffn(
    nc: bass.Bass,
    x: bass.AP,
    cond_8: bass.AP,
    skill_gate: bass.AP,
    skill_up: bass.AP,
    skill_down: bass.AP,
    shared_gate: bass.AP,
    shared_up: bass.AP,
    shared_down: bass.AP,
    Wp1: bass.AP,
    bp1: bass.AP,
    Wp2: bass.AP,
    bp2: bass.AP,
    W1: bass.AP,
    b1: bass.AP,
    W2: bass.AP,
    b2: bass.AP,
    Wo: bass.AP,
    bo: bass.AP,
    out: bass.AP,
):
    fp32 = mybir.dt.float32
    fp32r = mybir.dt.float32r
    u32 = mybir.dt.uint32
    ALU = mybir.AluOpType
    ACT = mybir.ActivationFunctionType
    AX = mybir.AxisListType

    P = 128
    B, S, H = x.shape
    E, _, I = skill_gate.shape
    F = W1.shape[2]
    KH = H // P
    HALF = S // 2
    IT = I // P
    FT = F // P
    TT = S // P
    TH = HALF // P
    CHUNKS = IT // 2
    CW = 2 * P
    PARTS = 2 * KH + 2
    STEPS = 3
    TILES = 2 * IT
    LAG = 2
    AHEAD = 2
    RING = 4
    TOP_K = 2
    SCALE = 1.0 / 12
    WARM = 4
    MIX = 0.3
    PIECES = 3
    assert PARTS == PIECES * KH and H == CW and HALF == 512 and TILES % RING == 0 and B * E <= P

    ctx = ExitStack()
    with ctx:
        ctx.enter_context(nc.allow_non_contiguous_dma(reason="biases onto partitions, a few KB"))

        def sb(name, shape, dt=fp32):
            return ctx.enter_context(nc.sbuf_tensor(name, shape, dt))

        def sem(name):
            return ctx.enter_context(nc.semaphore(name))

        w_raw = sb("w_raw", [P, CHUNKS, PARTS, CW])
        w_hi = sb("w_hi", [P, CHUNKS, PARTS, CW], fp32r)
        w_lo = sb("w_lo", [P, CHUNKS, PARTS, CW], fp32r)
        x_raw = sb("x_raw", [P, TT, H])
        xb = sb("xb", [P, TT, H])
        xT_hi = sb("xT_hi", [P, 2, KH, HALF], fp32r)
        xT_lo = sb("xT_lo", [P, 2, KH, HALF], fp32r)
        act = sb("act", [P, 2, HALF])
        h32 = sb("h32", [P, 2, HALF])
        h_hi = sb("h_hi", [P, RING, HALF], fp32r)
        h_lo = sb("h_lo", [P, RING, HALF], fp32r)
        c32 = sb("c32", [P, 2, KH, HALF])
        c_hi = sb("c_hi", [P, 2, KH, HALF], fp32r)
        c_lo = sb("c_lo", [P, 2, KH, HALF], fp32r)
        f_raw = sb("f_raw", [P, KH * F + FT * H])
        f_hi = sb("f_hi", [P, KH * F + FT * H], fp32r)
        f_lo = sb("f_lo", [P, KH * F + FT * H], fp32r)
        r_hi = sb("r_hi", [P, 2, KH, HALF], fp32r)
        r_lo = sb("r_lo", [P, 2, KH, HALF], fp32r)
        wo_raw = sb("wo_raw", [P, KH, H])
        wo_hi = sb("wo_hi", [P, KH, H], fp32r)
        wo_lo = sb("wo_lo", [P, KH, H], fp32r)
        ident = sb("ident", [P, P])
        zeros = sb("zeros", [P, HALF], mybir.dt.bfloat16)
        wp1 = sb("wp1", [P, KH, P])
        wp2 = sb("wp2", [P, E])
        bp1_c = sb("bp1_c", [P, 1])
        bp2_r = sb("bp2_r", [1, E])
        b1_c = sb("b1_c", [P, FT])
        b2_c = sb("b2_c", [P, KH])
        b2_m = sb("b2_m", [P, KH])
        bo_b = sb("bo_b", [P, H])
        bo_m = sb("bo_m", [P, H])
        logit = sb("logit", [P, B, E])
        top = sb("top", [P, B, 8])
        neg = sb("neg", [P, B])
        prob = sb("prob", [P, B, E])
        denom = sb("denom", [P, B])
        top_i = sb("top_i", [P, B, 8], u32)
        wsum = sb("wsum", [P, B])
        wnorm = sb("wnorm", [P, B, TOP_K])
        wmix = sb("wmix", [P, B, TOP_K])
        gain = sb("gain", [P, B * STEPS])
        nav = sb("nav", [P, 1])
        rl = sb("rl", [1, E])
        rtop = sb("rtop", [1, 8])
        rneg = sb("rneg", [1, 1])
        rexp = sb("rexp", [1, E])
        rsum = sb("rsum", [1, 1])
        rprob = sb("rprob", [1, E])
        rptop = sb("rptop", [1, 8])
        rsel = sb("rsel", [1, 8], u32)

        f1_hi = xT_hi[:, :, :, :].rearrange("p t k n -> p (t k) n")
        f1_lo = xT_lo[:, :, :, :].rearrange("p t k n -> p (t k) n")
        hf_hi = (h_hi, f1_hi)
        hf_lo = (h_lo, f1_lo)

        acc = ctx.enter_context(nc.psum_tensor("acc", [P, 2, KH, HALF], fp32))
        turn = ctx.enter_context(nc.psum_tensor("turn", [P, 4, HALF], fp32))

        cond_loaded = sem("cond_loaded")
        pool_consts_loaded = sem("pool_consts_loaded")
        router_loaded = sem("router_loaded")
        ident_step = sem("ident_step")
        ident_ready = sem("ident_ready")
        zeros_ready = sem("zeros_ready")
        wo_step = sem("wo_step")
        wo_split = sem("wo_split")
        route_dve = sem("route_dve")
        route_neg = sem("route_neg")
        route_exp = sem("route_exp")
        routed = sem("routed")
        x_loaded = [sem(f"x_loaded{t}") for t in range(2)]
        xb_ready = sem("xb_ready")
        x_transposed = sem("x_transposed")
        x_hi_done = sem("x_hi_done")
        x_split = sem("x_split")
        w_loaded = [[sem(f"w_loaded{c}_{i}") for i in range(PIECES)] for c in range(CHUNKS)]
        w_hi_done = sem("w_hi_done")
        w_split = sem("w_split")
        first_hi_done = sem("first_hi_done")
        gate_done = sem("gate_done")
        up_done = sem("up_done")
        gelu_done = sem("gelu_done")
        h_done = sem("h_done")
        h_hi_done = sem("h_hi_done")
        h_split = sem("h_split")
        down_done = sem("down_done")
        c_copied = sem("c_copied")
        c_hi_done = sem("c_hi_done")
        c_split = sem("c_split")
        c_turned = sem("c_turned")
        c_added = sem("c_added")
        nav_done = sem("nav_done")
        nav_gelu = sem("nav_gelu")
        rlogit_done = sem("rlogit_done")
        rneg_done = sem("rneg_done")
        rexp_done = sem("rexp_done")
        router_dve = sem("router_dve")
        waited_apart = sem("waited_apart")
        f_loaded = [sem("f1_loaded"), sem("f2_loaded")]
        fb_loaded = sem("fb_loaded")
        f_hi_done = sem("f_hi_done")
        f_split = sem("f_split")
        b2_done = sem("b2_done")
        inner_done = sem("inner_done")
        inner_gelu = sem("inner_gelu")
        inner_hi = sem("inner_hi")
        inner_split = sem("inner_split")
        r_done = sem("r_done")
        r_evac = sem("r_evac")
        r_hi_done = sem("r_hi_done")
        r_split = sem("r_split")
        sum_done = sem("sum_done")
        out_ready = sem("out_ready")
        out_stored = [sem(f"out_stored{q}") for q in range(4)]

        block = ctx.enter_context(nc.Block())

        def wait_apart(eng, semaphore, value):
            eng.wait_ge(semaphore, value)
            eng.sem_inc(waited_apart, 1)

        f_part = (slice(0, KH * F), slice(KH * F, KH * F + FT * H))
        half_of = lambda n: 1 - n // IT
        x_v = x.rearrange("b (t p) h -> b p t h", p=P)
        out_v = out.rearrange("b (t p) h -> b p t h", p=P)

        @block.sync
        def _(sp):
            def load_piece(c, i, w):
                src = (w[:, c * CW:(c + 1) * CW] if i < 2 else w[c * CW:(c + 1) * CW, :])
                sp.dma_start(w_raw[:, c, i * KH:(i + 1) * KH, :],
                             src.rearrange("(k p) n -> p k n", p=P)).then_inc(w_loaded[c][i], 16)

            def load_x(b, t):
                sp.dma_start(x_raw[:, t * TH:(t + 1) * TH, :],
                             x_v[b, :, t * TH:(t + 1) * TH, :]).then_inc(x_loaded[t], 16)

            def load_chunk(c, weights, step):
                for i, w in enumerate(weights):
                    if step is not None:
                        sp.wait_ge(w_split, PIECES * (CHUNKS * step + c) + i + 1)
                    load_piece(c, i, w)

            shared = (shared_gate, shared_up, shared_down)
            load_x(0, 1)
            load_piece(0, 0, shared_gate)
            load_x(0, 0)
            load_piece(0, 1, shared_up)
            load_piece(0, 2, shared_down)
            for c in range(1, CHUNKS):
                load_chunk(c, shared, None)
            sp.wait_ge(routed, 1)
            with sp.Fori(0, B) as b:
                with sp.Fori(0, TOP_K) as e:
                    k = sp.value_load(top_i[0:1, b, bass.ds(e, 1)], min_val=0, max_val=E - 1)
                    for c in range(CHUNKS):
                        load_chunk(c, (skill_gate[k, :, :], skill_up[k, :, :], skill_down[k, :, :]),
                                   STEPS * b + e)
                with sp.If(b < B - 1):
                    sp.wait_ge(x_transposed, 4 * b + 4)
                    sp.wait_ge(xb_ready, 4 * b + 4)
                    following = nc.s_assert_within(b + 1, 0, B - 1, skip_runtime_bounds_check_because="the If's condition")
                    load_x(following, 1)
                    load_x(following, 0)
                    for c in range(CHUNKS):
                        load_chunk(c, shared, STEPS * b + 2)
                sp.wait_ge(out_ready, 4 * b + 4)
                wait_apart(sp, router_dve, 6 * b + 6)
                k = sp.value_load(rsel[0:1, 0:1], min_val=0, max_val=E - 1)
                sp.dma_start(f_raw[:, 0:KH * F].rearrange("p (k n) -> p k n", k=KH),
                             W1[k, :, :].rearrange("(k p) n -> p k n", p=P)).then_inc(f_loaded[0], 16)
                sp.dma_start(b1_c[:, :], b1[k, :].rearrange("(f p) -> p f", p=P)).then_inc(fb_loaded, 16)
                sp.dma_start(f_raw[:, KH * F:].rearrange("p (k n) -> p k n", k=FT),
                             W2[k, :, :].rearrange("(k p) n -> p k n", p=P)).then_inc(f_loaded[1], 16)
                sp.dma_start(b2_c[:, :], b2[k, :].rearrange("(f p) -> p f", p=P)).then_inc(fb_loaded, 16)

        @block.gpsimd
        def _(pool):
            pool.memset(ident[:, :], 0.0).then_inc(ident_step, 1)
            pool.wait_ge(ident_step, 1)
            pool.affine_select(out=ident[:, :], in_=ident[:, :], compare_op=ALU.not_equal, fill=1.0,
                               base=0, pattern=[[-1, P]], channel_multiplier=1).then_inc(ident_ready, 1)
            pool.wait_ge(x_loaded[0], 16)
            pool.dma_start(wo_raw[:, :, :], Wo.rearrange("(k p) n -> p k n", p=P)).then_inc(pool_consts_loaded, 16)
            pool.dma_start(bo_b[:, :], bo.partition_broadcast(P)).then_inc(pool_consts_loaded, 16)
            pool.dma_start(wp1[:, :, :], Wp1.rearrange("(k p) n -> p k n", p=P)).then_inc(router_loaded, 16)
            pool.dma_start(wp2[:, :], Wp2).then_inc(router_loaded, 16)
            pool.dma_start(bp1_c[:, :], bp1.rearrange("(p o) -> p o", o=1)).then_inc(router_loaded, 16)
            pool.dma_start(bp2_r[:, :], bp2.rearrange("(o n) -> o n", o=1)).then_inc(router_loaded, 16)
            pool.wait_ge(pool_consts_loaded, 32)
            pool.tensor_scalar(bo_m[:, :], bo_b[:, :], MIX, None, ALU.mult).then_inc(wo_step, 1)
            pool.tensor_copy(wo_hi[:, :, :], wo_raw[:, :, :]).then_inc(wo_step, 1)
            pool.wait_ge(wo_step, 2)
            pool.tensor_tensor(wo_lo[:, :, :], wo_raw[:, :, :], wo_hi[:, :, :].bitcast(fp32),
                               ALU.subtract).then_inc(wo_split, 1)
            with pool.Fori(0, B) as b:
                for t in (1, 0):
                    pool.wait_ge(x_loaded[t], 16 * b + 16)
                    for q in (2 * t, 2 * t + 1):
                        pool.wait_ge(out_stored[q], 16 * b + 16)
                    for i in range(t * TH, (t + 1) * TH):
                        last = pool.tensor_tensor(xb[:, i, :], x_raw[:, i, :], bo_m[:, :], ALU.add)
                    last.then_inc(xb_ready, 2)

        @block.scalar
        def _(sc):
            sc.dma_start(logit[:, :, :], cond_8.partition_broadcast(P)).then_inc(cond_loaded, 16)
            sc.wait_ge(route_neg, 1)
            for b in range(B):
                last = sc.activation(prob[:, b, :], logit[:, b, :], ACT.Exp, bias=neg[:, b:b + 1])
            last.then_inc(route_exp, 1)

            def split_piece(b, j, c, i):
                sc.wait_ge(w_loaded[c][i], 16 * (STEPS * b + j + 1))
                if i == 0:
                    sc.wait_ge(down_done, TILES * (STEPS * b + j) + IT + 2 * c + 2)
                sc.activation(w_hi[:, c, i * KH:(i + 1) * KH, :], w_raw[:, c, i * KH:(i + 1) * KH, :],
                              ACT.Copy).then_inc(w_hi_done, 1)

            def split_chunk(b, j, c):
                for i in range(PIECES):
                    split_piece(b, j, c, i)

            def split_x(b, t):
                for k in range(KH):
                    sc.wait_ge(x_transposed, 4 * b + 2 * (1 - t) + k + 1)
                    sc.activation(xT_hi[:, t, k, :], acc[:, t, k, :], ACT.Copy).then_inc(x_hi_done, 1)

            def tile(b, j, n):
                done = TILES * (STEPS * b + j) + n
                sc.wait_ge(gate_done, done + 1)
                sc.wait_ge(h_done, done + 1)
                sc.activation(act[:, n % 2, :], turn[:, 2 * (n % 2), :], ACT.Gelu_apprx_tanh
                              ).then_inc(gelu_done, 1)

            def step(b, j, last=False):
                for n in range(TILES):
                    tile(b, j, n)
                    if n in (1, 3):
                        split_chunk(b, j, (n + 3) // 2)
                    if n in (13, 15):
                        if last:
                            with sc.If(b < B - 1):
                                split_chunk(b, j + 1, (n - 13) // 2)
                        else:
                            split_chunk(b, j + 1, (n - 13) // 2)
                    if last and n == IT + 2:
                        sc.wait_ge(router_loaded, 64)
                        sc.wait_ge(nav_done, b + 1)
                        sc.activation(nav[:, :], acc[:, 1, 0, 0:1], ACT.Gelu, bias=bp1_c[:, :]
                                      ).then_inc(nav_gelu, 1)
                        sc.wait_ge(rneg_done, b + 1)
                        sc.activation(rexp[:, :], rl[:, :], ACT.Exp, bias=rneg[:, :],
                                      accum_out=rsum[:, :]).then_inc(rexp_done, 1)
                    if last and n in (TILES - 2, TILES - 1):
                        i = n - (TILES - 2)
                        sc.wait_ge(f_loaded[i], 16 * b + 16)
                        sc.activation(f_hi[:, f_part[i]], f_raw[:, f_part[i]], ACT.Copy).then_inc(f_hi_done, 1)

            sc.sem_inc(gelu_done, AHEAD)
            for q in range(4):
                sc.sem_inc(out_stored[q], 16)
            split_x(0, 1)
            sc.sem_inc(w_hi_done, 1)
            split_piece(0, 0, 0, 1)
            split_x(0, 0)
            split_piece(0, 0, 0, 2)
            split_chunk(0, 0, 1)
            with sc.Fori(0, B) as b:
                with sc.Fori(0, STEPS - 1) as j:
                    step(b, j)
                step(b, STEPS - 1, last=True)
                sc.wait_ge(fb_loaded, 32 * b + 32)
                for u in range(2):
                    for f in range(FT):
                        i = u * FT + f
                        sc.wait_ge(inner_done, 2 * FT * b + i + 1)
                        if i < 2:
                            sc.wait_ge(h_done, TILES * STEPS * (b + 1) + AHEAD - 1 + i)
                        else:
                            sc.wait_ge(inner_split, 2 * FT * b + i - 1)
                        sc.activation(act[:, i % 2, :], turn[:, f, :], ACT.Gelu, bias=b1_c[:, f:f + 1]
                                      ).then_inc(inner_gelu, 1)
                sc.wait_ge(b2_done, b + 1)
                for u in range(2):
                    for m in range(KH):
                        i = u * KH + m
                        sc.wait_ge(r_done, 4 * b + i + 1)
                        if i < 2:
                            sc.wait_ge(inner_split, 2 * FT * b + 2 * FT - 1 + i)
                        else:
                            sc.wait_ge(r_split, 4 * b + i - 1)
                        sc.activation(act[:, i % 2, :], acc[:, 1 - u, m, :], ACT.Identity,
                                      bias=b2_m[:, m:m + 1], scale=MIX).then_inc(r_evac, 1)
                with sc.If(b < B - 1):
                    split_x(b + 1, 1)
                    split_x(b + 1, 0)
                for i, q in enumerate((2, 3, 0, 1)):
                    sc.wait_ge(out_ready, 4 * b + 4 + i + 1)
                    sc.dma_start(out_v[b, :, 2 * q:2 * q + 2, :], xb[:, 2 * q:2 * q + 2, :]
                                 ).then_inc(out_stored[q], 16)
            for q in range(4):
                sc.wait_ge(out_stored[q], 16 * B + 16)

        @block.vector
        def _(ve):
            ve.memset(zeros[:, :], 0.0).then_inc(zeros_ready, 1)
            ve.sem_inc(h_done, AHEAD)
            ve.sem_inc(out_ready, 4)
            ve.wait_ge(cond_loaded, 16)
            for b in range(B):
                ve.max(top[:, b, :], logit[:, b, :]).then_inc(route_dve, 1)
            ve.wait_ge(route_dve, B)
            ve.tensor_scalar(neg[:, :], top[:, :, 0], -1.0, None, ALU.mult).then_inc(route_neg, 1)

            def split_piece(b, j, c, i):
                ve.wait_ge(w_hi_done, PIECES * (CHUNKS * (STEPS * b + j) + c) + i + 1)
                part = slice(i * KH, (i + 1) * KH)
                ve.tensor_tensor(w_lo[:, c, part, :], w_raw[:, c, part, :],
                                 w_hi[:, c, part, :].bitcast(fp32), ALU.subtract).then_inc(w_split, 1)

            def split_x(b, t):
                for k in range(KH):
                    ve.wait_ge(x_hi_done, 4 * b + 2 * (1 - t) + k + 1)
                    ve.tensor_tensor(xT_lo[:, t, k, :], acc[:, t, k, :],
                                     xT_hi[:, t, k, :].bitcast(fp32), ALU.subtract).then_inc(x_split, 1)

            def split_chunk(b, j, c):
                for i in range(PIECES):
                    split_piece(b, j, c, i)

            def tile(b, j, n):
                done = TILES * (STEPS * b + j) + n
                ve.wait_ge(gelu_done, done + AHEAD + 1)
                ve.wait_ge(up_done, done + 1)
                s = n % 2
                ve.scalar_tensor_tensor(h32[:, s, :], act[:, s, :], gain[:, bass.ds(b * STEPS + j, 1)],
                                        turn[:, 2 * s + 1, :], ALU.mult, ALU.mult).then_inc(h_done, 1)
                ve.wait_ge(h_done, done + AHEAD + 1)
                ve.wait_ge(down_done, done + TILES - RING + 1)
                ve.tensor_copy(h_hi[:, n % RING, :], h32[:, s, :]).then_inc(h_hi_done, 1)
                ve.wait_ge(h_hi_done, done + 1)
                ve.tensor_tensor(h_lo[:, n % RING, :], h32[:, s, :], h_hi[:, n % RING, :].bitcast(fp32),
                                 ALU.subtract).then_inc(h_split, 1)

            def take_moe(b, u):
                t = 1 - u
                ve.wait_ge(down_done, TILES + TILES * STEPS * b + TILES * (STEPS - 1) + IT * (u + 1))
                ve.tensor_copy(c32[:, t, :, :], acc[:, t, :, :]).then_inc(c_copied, 1)
                ve.wait_ge(c_copied, 2 * b + u + 1)
                ve.tensor_copy(c_hi[:, t, :, :], c32[:, t, :, :]).then_inc(c_hi_done, 1)
                ve.wait_ge(c_hi_done, 2 * b + u + 1)
                ve.tensor_tensor(c_lo[:, t, :, :], c32[:, t, :, :], c_hi[:, t, :, :].bitcast(fp32),
                                 ALU.subtract).then_inc(c_split, 1)

            def add_moe(b, u):
                for i in range(2):
                    q = 2 * (1 - u) + i
                    ve.wait_ge(c_turned, 4 * b + 2 * u + i + 1)
                    ve.tensor_tensor(xb[:, 2 * q:2 * q + 2, :],
                                     acc[:, 1 - u, i, :].rearrange("p (t h) -> p t h", h=H),
                                     xb[:, 2 * q:2 * q + 2, :], ALU.add).then_inc(c_added, 1)

            def router_logits(b):
                ve.wait_ge(rlogit_done, b + 1)
                ve.tensor_tensor(rl[:, :], acc[0:1, 1, 1, 0:E], bp2_r[:, :], ALU.add).then_inc(router_dve, 1)
                wait_apart(ve, router_dve, 6 * b + 1)
                ve.max(rtop[:, :], rl[:, :]).then_inc(router_dve, 1)
                ve.wait_ge(router_dve, 6 * b + 2)
                ve.tensor_scalar(rneg[:, :], rtop[:, 0:1], -1.0, None, ALU.mult).then_inc(rneg_done, 1)

            def router_choice(b):
                ve.wait_ge(rexp_done, b + 1)
                ve.reciprocal(rsum[:, :], rsum[:, :]).then_inc(router_dve, 1)
                ve.wait_ge(router_dve, 6 * b + 3)
                ve.tensor_scalar(rprob[:, :], rexp[:, :], rsum[:, :], None, ALU.mult).then_inc(router_dve, 1)
                wait_apart(ve, router_dve, 6 * b + 4)
                ve.max(rptop[:, :], rprob[:, :]).then_inc(router_dve, 1)
                wait_apart(ve, router_dve, 6 * b + 5)
                ve.max_index(rsel[:, :], rptop[:, :], rprob[:, :]).then_inc(router_dve, 1)

            def step(b, j, last=False):
                for n in range(TILES):
                    tile(b, j, n)
                    if n in (1, 3):
                        split_chunk(b, j, (n + 3) // 2)
                    if n in (13, 15):
                        if last:
                            with ve.If(b < B - 1):
                                split_chunk(b, j + 1, (n - 13) // 2)
                        else:
                            split_chunk(b, j + 1, (n - 13) // 2)
                    if last and n == IT + 1:
                        take_moe(b, 0)
                    if last and n == IT + 2:
                        router_logits(b)
                    if last and n == IT + 3:
                        router_choice(b)
                    if last and n == IT + 4:
                        ve.wait_ge(xb_ready, 4 * b + 4)
                        add_moe(b, 0)
                    if last and n in (TILES - 2, TILES - 1):
                        i = n - (TILES - 2)
                        ve.wait_ge(f_hi_done, 2 * b + i + 1)
                        ve.tensor_tensor(f_lo[:, f_part[i]], f_raw[:, f_part[i]],
                                         f_hi[:, f_part[i]].bitcast(fp32), ALU.subtract).then_inc(f_split, 1)

            ve.wait_ge(w_loaded[0][0], 16)
            ve.tensor_copy(w_hi[:, 0, 0:KH, :], w_raw[:, 0, 0:KH, :]).then_inc(first_hi_done, 1)
            ve.wait_ge(first_hi_done, 1)
            ve.tensor_tensor(w_lo[:, 0, 0:KH, :], w_raw[:, 0, 0:KH, :], w_hi[:, 0, 0:KH, :].bitcast(fp32),
                             ALU.subtract).then_inc(w_split, 1)
            split_x(0, 1)
            split_piece(0, 0, 0, 1)
            split_x(0, 0)
            ve.memset(gain[:, :], 1.0).then_inc(route_dve, 1)
            ve.wait_ge(route_exp, 1)
            ve.reduce_sum(denom[:, :], prob[:, :, :], AX.X).then_inc(route_dve, 1)
            ve.wait_ge(route_dve, B + 2)
            ve.reciprocal(denom[:, :], denom[:, :]).then_inc(route_dve, 1)
            ve.wait_ge(route_dve, B + 3)
            ve.tensor_tensor(prob[:, :, :], prob[:, :, :], denom[:, :].unsqueeze(2).broadcast_to([P, B, E]),
                             ALU.mult).then_inc(route_dve, 1)
            ve.wait_ge(route_dve, B + 4)
            for b in range(B):
                ve.max(top[:, b, :], prob[:, b, :]).then_inc(route_dve, 1)
            ve.wait_ge(route_dve, 2 * B + 4)
            for b in range(B):
                ve.max_index(top_i[:, b, :], top[:, b, :], prob[:, b, :]).then_inc(route_dve, 1)
            ve.reduce_sum(wsum[:, :], top[:, :, 0:TOP_K], AX.X).then_inc(route_dve, 1)
            ve.wait_ge(route_dve, 3 * B + 5)
            ve.reciprocal(wsum[:, :], wsum[:, :]).then_inc(route_dve, 1)
            ve.wait_ge(route_dve, 3 * B + 6)
            ve.tensor_tensor(wnorm[:, :, :], top[:, :, 0:TOP_K],
                             wsum[:, :].unsqueeze(2).broadcast_to([P, B, TOP_K]),
                             ALU.mult).then_inc(route_dve, 1)
            ve.wait_ge(route_dve, 3 * B + 7)
            ve.tensor_scalar(wmix[:, :, :], wnorm[:, :, :], 1.0 - SCALE, None, ALU.mult).then_inc(route_dve, 1)
            ve.wait_ge(route_dve, 3 * B + 8)
            ve.scalar_tensor_tensor(gain[:, :].rearrange("p (b j) -> p b j", b=B)[:, :, 1:1 + TOP_K],
                                    wnorm[:, :, :], SCALE, wmix[:, :, :], ALU.mult, ALU.add).then_inc(routed, 1)
            ve.wait_ge(routed, 1)
            split_piece(0, 0, 0, 2)
            split_chunk(0, 0, 1)
            with ve.Fori(0, B) as b:
                with ve.Fori(0, STEPS - 1) as j:
                    step(b, j)
                step(b, STEPS - 1, last=True)
                take_moe(b, 1)
                for u in range(2):
                    t = 1 - u
                    for f in range(FT):
                        i = u * FT + f
                        ve.wait_ge(inner_gelu, 2 * FT * b + i + 1)
                        ve.tensor_copy(hf_hi[t][:, f, :], act[:, i % 2, :]).then_inc(inner_hi, 1)
                        ve.wait_ge(inner_hi, 2 * FT * b + i + 1)
                        ve.tensor_tensor(hf_lo[t][:, f, :], act[:, i % 2, :], hf_hi[t][:, f, :].bitcast(fp32),
                                         ALU.subtract).then_inc(inner_split, 1)
                    if u == 0:
                        add_moe(b, 1)
                        ve.wait_ge(fb_loaded, 32 * b + 32)
                        ve.tensor_scalar(b2_m[:, :], b2_c[:, :], MIX, None, ALU.mult).then_inc(b2_done, 1)
                for u in range(2):
                    t = 1 - u
                    for m in range(KH):
                        i = u * KH + m
                        ve.wait_ge(r_evac, 4 * b + i + 1)
                        ve.tensor_copy(r_hi[:, t, m, :], act[:, i % 2, :]).then_inc(r_hi_done, 1)
                        ve.wait_ge(r_hi_done, 4 * b + i + 1)
                        ve.tensor_tensor(r_lo[:, t, m, :], act[:, i % 2, :], r_hi[:, t, m, :].bitcast(fp32),
                                         ALU.subtract).then_inc(r_split, 1)
                ve.wait_ge(c_added, 4 * b + 4)
                for i, q in enumerate((2, 3, 0, 1)):
                    if i == 2:
                        with ve.If(b < B - 1):
                            split_x(b + 1, 1)
                    ve.wait_ge(sum_done, 4 * b + i + 1)
                    ve.tensor_tensor(xb[:, 2 * q:2 * q + 2, :],
                                     turn[:, i, :].rearrange("p (t h) -> p t h", h=H),
                                     xb[:, 2 * q:2 * q + 2, :], ALU.add).then_inc(out_ready, 1)
                with ve.If(b < B - 1):
                    split_x(b + 1, 0)

        @block.tensor
        def _(pe):
            def product(o, terms, start, stop):
                passes = [(l, r) for lh, ll, rh, rl_ in terms for l, r in ((ll, rh), (lh, rl_), (lh, rh))]
                for i, (l, r) in enumerate(passes):
                    ins = pe.matmul(o, l, r, start=start and i == 0, stop=stop and i == len(passes) - 1,
                                    skip_group_check=True)
                return ins

            def gate_up(b, j, n):
                done = TILES * (STEPS * b + j) + n
                c, i, t, s = n % IT // 2, n % 2, half_of(n), n % 2
                for part, ready, free in ((0, gate_done, gelu_done), (1, up_done, h_done)):
                    if n < IT and n % 2 == 0:
                        pe.wait_ge(w_split, PIECES * (CHUNKS * (STEPS * b + j) + c) + part + 1)
                    pe.wait_ge(free, done + 1)
                    product(turn[:, 2 * s + part, :],
                            [(w_hi[:, c, part * KH + k, i * P:(i + 1) * P],
                              w_lo[:, c, part * KH + k, i * P:(i + 1) * P],
                              xT_hi[:, t, k, :], xT_lo[:, t, k, :]) for k in range(KH)],
                            True, True).then_inc(ready, 1)

            def down(b, j, n, stop=False):
                c, i, t = n % IT // 2, n % 2, half_of(n)
                pe.wait_ge(h_split, TILES * (STEPS * b + j) + n + 1)
                if n < IT and n % 2 == 0:
                    pe.wait_ge(w_split, PIECES * (CHUNKS * (STEPS * b + j) + c) + PIECES)
                for m in range(KH):
                    last = product(acc[:, t, m, :],
                                   [(w_hi[:, c, 2 * KH + i, m * P:(m + 1) * P],
                                     w_lo[:, c, 2 * KH + i, m * P:(m + 1) * P],
                                     h_hi[:, n % RING, :], h_lo[:, n % RING, :])], False, stop)
                last.then_inc(down_done, 1)

            def inner(b, u, f):
                t = 1 - u
                pe.wait_ge(c_split, 2 * b + u + 1)
                if u:
                    pe.wait_ge(inner_gelu, 2 * FT * b + f + 1)
                else:
                    pe.wait_ge((gelu_done, h_done)[f % 2], TILES * STEPS * (b + 1) + AHEAD - 1 + f // 2)
                product(turn[:, f, :],
                        [(f_hi[:, k * F + f * P:k * F + (f + 1) * P],
                          f_lo[:, k * F + f * P:k * F + (f + 1) * P],
                          c_hi[:, t, k, :], c_lo[:, t, k, :]) for k in range(KH)],
                        True, True).then_inc(inner_done, 1)

            def turn_c(b, u):
                t = 1 - u
                for i in range(TH):
                    for k in range(KH):
                        last = pe.transpose(acc[:, t, i // 2, i % 2 * H + k * P:i % 2 * H + (k + 1) * P],
                                            c32[:, t, k, i * P:(i + 1) * P], ident[:, :])
                    if i % 2:
                        last.then_inc(c_turned, 1)

            def outer(b, u, m):
                t = 1 - u
                if m == 0:
                    pe.wait_ge(c_added, 4 * b + 2 * (u + 1))
                pe.wait_ge(inner_split, 2 * FT * b + FT * (u + 1))
                product(acc[:, t, m, :],
                        [(f_hi[:, KH * F + k * H + m * P:KH * F + k * H + (m + 1) * P],
                          f_lo[:, KH * F + k * H + m * P:KH * F + k * H + (m + 1) * P],
                          hf_hi[t][:, k, :], hf_lo[t][:, k, :]) for k in range(FT)],
                        True, True).then_inc(r_done, 1)

            def final(b, u, q):
                t = 1 - u
                bank = 2 * u + q % 2
                pe.wait_ge(r_split, 4 * b + 2 * (u + 1))
                pe.wait_ge(inner_gelu, 2 * FT * b + FT + bank + 1)
                for i in range(2):
                    tok = slice((2 * (q % 2) + i) * P, (2 * (q % 2) + i + 1) * P)
                    last = product(turn[:, bank, i * H:(i + 1) * H],
                                   [(r_hi[:, t, k, tok], r_lo[:, t, k, tok], wo_hi[:, k, :], wo_lo[:, k, :])
                                    for k in range(KH)], True, True)
                last.then_inc(sum_done, 1)

            def turn_x(b, t):
                pe.wait_ge(x_loaded[t], 16 * b + 16)
                for k in range(KH):
                    for i in range(TH):
                        last = pe.transpose(acc[:, t, k, i * P:(i + 1) * P],
                                            x_raw[:, t * TH + i, k * P:(k + 1) * P], ident[:, :])
                    last.then_inc(x_transposed, 1)

            def clear(t, columns=2):
                for m in range(KH):
                    pe.matmul(acc[:, t, m, 0:columns], zeros[:, 0:P], zeros[:, 0:columns], start=True,
                              stop=False, skip_group_check=True)

            pe.sem_inc(down_done, TILES)
            pe.wait_ge(zeros_ready, 1)
            for _ in range(WARM):
                clear(1, HALF)
            pe.wait_ge(ident_ready, 1)
            turn_x(0, 1)
            turn_x(0, 0)
            with pe.Fori(0, B) as b:
                pe.wait_ge(x_split, 4 * b + KH)
                clear(1)
                pe.wait_ge(out_ready, 4 * b + 2)
                gate_up(b, 0, 0)
                pe.wait_ge(x_split, 4 * b + 2 * KH)
                clear(0)
                pe.wait_ge(out_ready, 4 * b + 4)
                gate_up(b, 0, 1)
                with pe.Fori(0, STEPS - 1) as j:
                    for n in range(LAG, TILES):
                        gate_up(b, j, n)
                        down(b, j, n - LAG)
                    for n in range(LAG):
                        gate_up(b, j + 1, n)
                        down(b, j, TILES - LAG + n)
                for n in range(LAG, TILES):
                    gate_up(b, STEPS - 1, n)
                    if n == IT + 2:
                        pe.wait_ge(c_copied, 2 * b + 1)
                        pe.wait_ge(router_loaded, 64)
                        for k in range(KH):
                            last = pe.matmul(acc[:, 1, 0, 0:1], wp1[:, k, :], c32[:, 1, k, HALF - 1:HALF],
                                             start=k == 0, stop=k == KH - 1, skip_group_check=True)
                        last.then_inc(nav_done, 1)
                    if n == IT + 3:
                        pe.wait_ge(nav_gelu, b + 1)
                        pe.matmul(acc[0:1, 1, 1, 0:E], nav[:, :], wp2[:, :], start=True, stop=True,
                                  skip_group_check=True).then_inc(rlogit_done, 1)
                    if n == IT + 4:
                        pe.wait_ge(router_dve, 6 * b + 1)
                        turn_c(b, 0)
                    down(b, STEPS - 1, n - LAG, stop=n - LAG in (IT - 1, TILES - 1))
                for n in range(TILES - LAG, TILES):
                    down(b, STEPS - 1, n, stop=n == TILES - 1)
                pe.wait_ge(f_split, 2 * b + 1)
                for f in range(FT):
                    inner(b, 0, f)
                pe.wait_ge(c_copied, 2 * b + 2)
                turn_c(b, 1)
                for f in range(FT):
                    inner(b, 1, f)
                pe.wait_ge(f_split, 2 * b + 2)
                for u in range(2):
                    for m in range(KH):
                        outer(b, u, m)
                pe.wait_ge(wo_split, 1)
                for u in range(2):
                    t = 1 - u
                    for q in (2 * t, 2 * t + 1):
                        final(b, u, q)
                    with pe.If(b < B - 1):
                        pe.wait_ge(r_evac, 4 * b + 2 * (u + 1))
                        turn_x(b + 1, t)


_INS = ["x", "cond_8", "L0_cond_skill_gate", "L0_cond_skill_up", "L0_cond_skill_down",
        "L0_cond_shared_gate", "L0_cond_shared_up", "L0_cond_shared_down",
        "L0_ffn_Wp1", "L0_ffn_bp1", "L0_ffn_Wp2", "L0_ffn_bp2", "L0_ffn_W1", "L0_ffn_b1",
        "L0_ffn_W2", "L0_ffn_b2", "L0_ffn_Wo", "L0_ffn_bo"]
_OUTS = [((2, 1024, 256), "float32")]


def kernel(**inputs):
    import numpy as _np
    import concourse.bacc as _bacc
    from concourse import mybir as _mybir
    from concourse.bass_utils import run_bass_kernel_spmd as _run

    nc = _bacc.Bacc("TRN2", target_bir_lowering=False, num_devices=1)
    arrays, args = {}, []
    for name in _INS:
        a = _np.ascontiguousarray(inputs[name])
        arrays[f"in_{name}_dram"] = a
        args.append(nc.dram_tensor(f"in_{name}_dram", a.shape, _mybir.dt.from_np(a.dtype), kind="ExternalInput").ap())
    for i, (shape, dtype) in enumerate(_OUTS):
        dt = _mybir.dt.from_np(_np.dtype(dtype))
        args.append(nc.dram_tensor(f"out_{i}_dram", shape, dt, kind="ExternalOutput").ap())
    adaln_moe_ffn(nc, *args)
    r = _run(nc, [arrays], core_ids=[0])
    return r.results[0]["out_0_dram"]
```
